# Optimizing a Trainium2 kernel written in Bass

```python
import numpy as np
import jax
import jax.numpy as jnp

def _softmax(x, axis=-1):
    return jax.nn.softmax(x, axis=axis)
def _gelu(x):
    return jax.nn.gelu(x, approximate=True)
def _silu(x):
    return jax.nn.silu(x)
def _sigmoid(x):
    return jax.nn.sigmoid(x)
def _layernorm(x, axis=-1, eps=1e-5):
    m = jnp.mean(x, axis=axis, keepdims=True)
    v = jnp.var(x, axis=axis, keepdims=True)
    return (x - m) / jnp.sqrt(v + eps)
def _scatter_add(tgt, idx, src, axis=0):
    return tgt.at[idx].add(src)
def _segment_sum(src, seg, n):
    return jax.ops.segment_sum(src, seg, n)

kernel_name = 'mk_conv_seq_d1_conv_nchw256_1ffa40'

def setup_inputs(seed: int = 0):
    np.random.seed(seed)
    _w = jnp.asarray
    def _rec_inputs():
        import jax
        import jax.numpy as jnp
        _gk = jax.random.key(seed)
        x = -7.109e-05 + 0.9999 * jax.random.normal(jax.random.fold_in(_gk, 1), (16, 256, 128, 128), jnp.float32)
        return x
    x = _rec_inputs()
    def _L0_conv_setup():
        import jax, jax.numpy as jnp
        import numpy as np
        B, C, H, W, K = (16, 256, 128, 128, 64)
        BN_EPS = 1e-05
        L1_EPS = 1e-06

        def _conv1x1(x, w, b):
            return jnp.einsum('bchw,kc->bkhw', x, w) + b[None, :, None, None]

        def _bn_lrelu(x, g, be, m, v):
            scale = g / jnp.sqrt(v + BN_EPS)
            x = (x - m[None, :, None, None]) * scale[None, :, None, None] + be[None, :, None, None]
            return jnp.where(x > 0, x, 0.1 * x)
        key = jax.random.key(seed)
        ks = jax.random.split(key, 24)
        d = {}
        d['x'] = jax.random.normal(ks[0], (B, C, H, W), jnp.float32)
        d['w0'] = jax.random.normal(ks[1], (K, C), jnp.float32) * 0.05
        d['b0'] = jax.random.normal(ks[2], (K,), jnp.float32) * 0.01
        d['g0'] = 1.0 + 0.1 * jax.random.normal(ks[3], (K,), jnp.float32)
        d['be0'] = jax.random.normal(ks[4], (K,), jnp.float32) * 0.01
        d['m0'] = jax.random.normal(ks[5], (K,), jnp.float32) * 0.1
        d['v0'] = 0.5 + jax.random.uniform(ks[6], (K,), jnp.float32)
        d['w1'] = jax.random.normal(ks[7], (K, K), jnp.float32) * 0.1
        d['b1'] = jax.random.normal(ks[8], (K,), jnp.float32) * 0.01
        d['g1'] = 1.0 + 0.1 * jax.random.normal(ks[9], (K,), jnp.float32)
        d['be1'] = jax.random.normal(ks[10], (K,), jnp.float32) * 0.01
        d['m1'] = jax.random.normal(ks[11], (K,), jnp.float32) * 0.1
        d['v1'] = 0.5 + jax.random.uniform(ks[12], (K,), jnp.float32)
        d['w2'] = jax.random.normal(ks[13], (K, K), jnp.float32) * 0.1
        d['b2'] = jax.random.normal(ks[14], (K,), jnp.float32) * 0.01
        d['g2'] = 1.0 + 0.1 * jax.random.normal(ks[15], (K,), jnp.float32)
        d['be2'] = jax.random.normal(ks[16], (K,), jnp.float32) * 0.01
        d['m2'] = jax.random.normal(ks[17], (K,), jnp.float32) * 0.1
        d['v2'] = 0.5 + jax.random.uniform(ks[18], (K,), jnp.float32)
        return d
    _L0_conv_all = _L0_conv_setup()
    _L0_conv_in = {k: v for k, v in _L0_conv_all.items() if k in ('w0', 'b0', 'g0', 'be0', 'm0', 'v0', 'w1', 'b1', 'g1', 'be1', 'm1', 'v1', 'w2', 'b2', 'g2', 'be2', 'm2', 'v2', )}
    del _L0_conv_all

    return {
        "x": x,
        "L0_conv_w0": _L0_conv_in["w0"],
        "L0_conv_b0": _L0_conv_in["b0"],
        "L0_conv_g0": _L0_conv_in["g0"],
        "L0_conv_be0": _L0_conv_in["be0"],
        "L0_conv_m0": _L0_conv_in["m0"],
        "L0_conv_v0": _L0_conv_in["v0"],
        "L0_conv_w1": _L0_conv_in["w1"],
        "L0_conv_b1": _L0_conv_in["b1"],
        "L0_conv_g1": _L0_conv_in["g1"],
        "L0_conv_be1": _L0_conv_in["be1"],
        "L0_conv_m1": _L0_conv_in["m1"],
        "L0_conv_v1": _L0_conv_in["v1"],
        "L0_conv_w2": _L0_conv_in["w2"],
        "L0_conv_b2": _L0_conv_in["b2"],
        "L0_conv_g2": _L0_conv_in["g2"],
        "L0_conv_be2": _L0_conv_in["be2"],
        "L0_conv_m2": _L0_conv_in["m2"],
        "L0_conv_v2": _L0_conv_in["v2"],
    }

def reference(x, L0_conv_w0, L0_conv_b0, L0_conv_g0, L0_conv_be0, L0_conv_m0, L0_conv_v0, L0_conv_w1, L0_conv_b1, L0_conv_g1, L0_conv_be1, L0_conv_m1, L0_conv_v1, L0_conv_w2, L0_conv_b2, L0_conv_g2, L0_conv_be2, L0_conv_m2, L0_conv_v2):
    import jax
    import jax.numpy as jnp
    def _L0_conv_ref(x, w0, b0, g0, be0, m0, v0, w1, b1, g1, be1, m1, v1, w2, b2, g2, be2, m2, v2):
        import jax, jax.numpy as jnp
        import numpy as np
        B, C, H, W, K = (16, 256, 128, 128, 64)
        BN_EPS = 1e-05
        L1_EPS = 1e-06

        def _conv1x1(x, w, b):
            return jnp.einsum('bchw,kc->bkhw', x, w) + b[None, :, None, None]

        def _bn_lrelu(x, g, be, m, v):
            scale = g / jnp.sqrt(v + BN_EPS)
            x = (x - m[None, :, None, None]) * scale[None, :, None, None] + be[None, :, None, None]
            return jnp.where(x > 0, x, 0.1 * x)
        residual = _bn_lrelu(_conv1x1(x, w0, b0), g0, be0, m0, v0)
        out = _bn_lrelu(_conv1x1(residual, w1, b1), g1, be1, m1, v1)
        out = _bn_lrelu(_conv1x1(out, w2, b2), g2, be2, m2, v2)
        sub = out + residual
        b_, c_, h_, w_ = x.shape
        hw = h_ * w_
        Vt = sub.reshape(b_, K, hw)
        Vt = Vt / (L1_EPS + jnp.sum(jnp.abs(Vt), axis=2, keepdims=True))
        mat = jnp.einsum('bkn,bjn->bkj', Vt, Vt)
        mat_inv = jnp.linalg.inv(mat)
        proj = jnp.einsum('bkj,bjn->bkn', mat_inv, Vt)
        xf = x.reshape(b_, c_, hw)
        pf = jnp.einsum('bkn,bcn->bkc', proj, xf)
        out = jnp.einsum('bkn,bkc->bcn', Vt, pf)
        return out.reshape(b_, c_, h_, w_)

    def _gn(v, G=32, eps=1e-5):
        B_, C_, H_, W_ = v.shape
        g = v.reshape(B_, G, C_ // G, H_, W_)
        m = jnp.mean(g, axis=(2, 3, 4), keepdims=True)
        s = jnp.var(g, axis=(2, 3, 4), keepdims=True)
        return ((g - m) / jnp.sqrt(s + eps)).reshape(v.shape)

    def _ln_c(v, eps=1e-6):
        m = jnp.mean(v, axis=1, keepdims=True)
        s = jnp.var(v, axis=1, keepdims=True)
        return (v - m) / jnp.sqrt(s + eps)

    def _ln_t(v, eps=1e-5):
        m = jnp.mean(v, axis=-1, keepdims=True)
        s = jnp.var(v, axis=-1, keepdims=True)
        return (v - m) / jnp.sqrt(s + eps)

    def _to_tokens(v):
        B_, C_, H_, W_ = v.shape
        return v.reshape(B_, C_, H_ * W_).transpose(0, 2, 1)
    def _from_tokens(t, like):
        B_, C_, H_, W_ = like.shape
        return t.transpose(0, 2, 1).reshape(B_, C_, H_, W_)

    x = _L0_conv_ref(x, L0_conv_w0, L0_conv_b0, L0_conv_g0, L0_conv_be0, L0_conv_m0, L0_conv_v0, L0_conv_w1, L0_conv_b1, L0_conv_g1, L0_conv_be1, L0_conv_m1, L0_conv_v1, L0_conv_w2, L0_conv_b2, L0_conv_g2, L0_conv_be2, L0_conv_m2, L0_conv_v2)
    return x


_drawn_inputs = setup_inputs


def setup_inputs(seed=0):
    import zlib

    import numpy as np

    out = dict(_drawn_inputs(seed))
    spreads = {}
    factors = {'L0_conv_b0': 7.321,
     'L0_conv_be0': 7.379,
     'L0_conv_b1': 8.0,
     'L0_conv_be1': 8.0,
     'L0_conv_b2': 7.833,
     'L0_conv_g2': 3.878,
     'L0_conv_be2': 7.045,
     'L0_conv_v2': 2.887}
    for name, (base, spread) in spreads.items():
        noise = np.random.default_rng([zlib.crc32(name.encode()), seed]).standard_normal(out[name].shape)
        drawn = base * np.exp(spread * noise) if base else spread * noise
        out[name] = jnp.asarray(drawn.astype(out[name].dtype))
    for name, factor in factors.items():
        out[name] = (out[name] * factor).astype(out[name].dtype)
    return out
```

```python
from contextlib import ExitStack

import concourse.bass as bass
from concourse import mybir

F32 = mybir.dt.float32
F32R = mybir.dt.float32r
ACT = mybir.ActivationFunctionType
ALU = mybir.AluOpType
AX = mybir.AxisListType

P = 128
BN_EPS = 1e-5
L1_EPS = 1e-6
SLOPE = 0.1

SUM_HALVES, TURN_GRAM, TURN_SCALED, FIRST_POWER = 0, 1, 2, 3
POWERS = 24
FIRST_FIX = FIRST_POWER + POWERS
FIXES = 3
PROJECT = FIRST_FIX + 2 * FIXES
SLOTS = PROJECT + 1
CHAIN = 8


def projection_kernel(nc, x, layers, out):
    B, C, H, W = x.shape
    K = layers[0]["w"].shape[0]
    N = H * W
    HALF = N // 2
    CH = 512
    STEPS = HALF // CH
    UNITS = STEPS // 2
    CT = C // P
    Q = CH // P
    GW = C + K
    assert K == 64 and CT == 2 and UNITS == 8 and Q == 4

    x_view = x.rearrange("b (ct c) h w -> b c ct (h w)", ct=CT)
    out_view = out.rearrange("b (ct c) h w -> b c ct (h w)", ct=CT)

    with ExitStack() as ctx:
        def sb(name, shape, dt=F32):
            return ctx.enter_context(nc.sbuf_tensor(name, shape, dt))

        def sem(name):
            return ctx.enter_context(nc.semaphore(name))

        ident = sb("ident", [P, P])
        fold = sb("fold", [P, K])
        spread = sb("spread", [P, P])
        minus_half = sb("minus_half", [P, 3])
        vec_rows = sb("vec_rows", [15, P])
        vecs = sb("vecs", [P, 5, 3])
        bn_scale = sb("bn_scale", [P, 3])
        bn_bias = sb("bn_bias", [P, 3])
        bn_tmp = sb("bn_tmp", [P, 2, 3])
        w0 = sb("w0", [K, C])
        w12 = sb("w12", [P, 2, P])
        w0T = sb("w0T", [P, CT, K])
        w12T = sb("w12T", [P, 2, P])

        xs = sb("xs", [P, 2, CT, 2, CH])
        y = sb("y", [P, 3, CH])
        r = sb("r", [P, 2, CH])
        o1 = sb("o1", [P, CH])
        o2 = sb("o2", [P, 2, CH])
        s_now = sb("s_now", [P, 2, CH])
        s_all = sb("s_all", [P, 2 * STEPS * CH])
        abs_out = sb("abs_out", [P, CH])
        l1_parts = sb("l1_parts", [P, 2 * STEPS])
        turned = sb("turned", [P, 2, Q, 2, GW])
        gram_s = sb("gram_s", [P, GW + 2])
        gram = sb("gram", [K, GW + 2])
        l1e = sb("l1e", [K, 1])
        d = sb("d", [K, 1])
        row_sums = sb("row_sums", [K, 1])
        e = sb("e", [K, 1])
        de = sb("de", [K, 1])
        amat = sb("amat", [K, K])
        square = sb("square", [P, K])
        scaled = sb("scaled", [P, K])
        powers = sb("powers", [P, 2, 2 * K])
        target = sb("target", [P, C])
        proj = sb("proj", [P, C])
        proj_hi = sb("proj_hi", [P, C], F32R)
        proj_lo = sb("proj_lo", [P, C], F32R)
        s_split = sb("s_split", [P, 2, 2, CH], F32R)
        out_s = sb("out_s", [P, 2, 2, CT, CH])

        gram_ps = ctx.enter_context(nc.psum_tensor("gram_ps", [P, CH], F32))
        conv_ps = ctx.enter_context(nc.psum_tensor("conv_ps", [P, 2, CH], F32))
        turn_ps = ctx.enter_context(nc.psum_tensor("turn_ps", [P, 2, CH], F32))
        out_ps = ctx.enter_context(nc.psum_tensor("out_ps", [P, 2, CH], F32))
        inv_ps = ctx.enter_context(nc.psum_tensor("inv_ps", [P, CH], F32))

        weights_loaded = sem("weights_loaded")
        vecs_loaded = sem("vecs_loaded")
        rows_doubled = sem("rows_doubled")
        vecs_turned = sem("vecs_turned")
        w12_zeroed = sem("w12_zeroed")
        ident_zeroed = sem("ident_zeroed")
        ident_ready = sem("ident_ready")
        var_ready = sem("var_ready")
        root_ready = sem("root_ready")
        const_step = sem("const_step")
        const_ready = sem("const_ready")
        weights_turned = sem("weights_turned")
        weights_ready = sem("weights_ready")
        x_loaded = [sem("x_loaded0"), sem("x_loaded1")]
        conv_ready = [sem(f"conv{i}_ready") for i in range(3)]
        y_ready = [sem(f"y{i}_ready") for i in range(3)]
        act_ready = [sem(f"act{i}_ready") for i in range(3)]
        s_ready = sem("s_ready")
        s_kept = sem("s_kept")
        abs_done = sem("abs_done")
        x_turned = sem("x_turned")
        x_evac_dve = sem("x_evac_dve")
        x_evac_act = sem("x_evac_act")
        s_turned = sem("s_turned")
        s_evac = sem("s_evac")
        gram_done = sem("gram_done")
        gram_saved = sem("gram_saved")
        inv_operand = sem("inv_operand")
        inv_product = sem("inv_product")
        inv_step = sem("inv_step")
        rows_summed = sem("rows_summed")
        rows_rooted = sem("rows_rooted")
        proj_ready = sem("proj_ready")
        proj_spread = sem("proj_spread")
        proj_hi_ready = sem("proj_hi_ready")
        proj_split = sem("proj_split")
        split_hi = sem("split_hi")
        split_done = sem("split_done")
        out_ready = [sem("out_ready0"), sem("out_ready1")]
        out_evac = [sem("out_evac0"), sem("out_evac1")]
        out_stored = [[sem(f"out_stored{s}{h}") for h in range(2)] for s in range(2)]

        block = ctx.enter_context(nc.Block())

        def wait(eng, s, value):
            if not isinstance(value, int) or value > 0:
                eng.wait_ge(s, value)

        def run(eng, unit):
            unit(0, 0, "first", True, False, False)
            with eng.Fori(1, UNITS) as u:
                unit(0, u, "mid", True, False, False)
            image(eng, unit, 1, True, True, False)
            image(eng, unit, 2, True, True, True)
            with eng.Fori(3, B) as b:
                image(eng, unit, b, True, True, True)
            image(eng, unit, B, False, True, True)
            image(eng, unit, B + 1, False, False, True)

        def image(eng, unit, b, feats, inv, outs):
            unit(b, 0, "first", feats, inv, outs)
            with eng.Fori(1, UNITS - 1) as u:
                unit(b, u, "mid", feats, inv, outs)
            unit(b, UNITS - 1, "last", feats, inv, outs)

        def slots_of(kind, u, s):
            if kind == "first":
                return {1: SUM_HALVES, 2: TURN_GRAM, 3: TURN_SCALED} if s else {}
            if kind == "mid":
                at = FIRST_POWER + 4 * (u - 1) + 2 * s
                return {1: at, 3: at + 1}
            at = FIRST_FIX + 4 * s
            return {place: at + place for place in range(4) if at + place < SLOTS}

        def turns_last(b, kind, s, feats):
            first = kind == "first" and s == 0
            return (feats or first and isinstance(b, int) and b == B) and not (
                first and isinstance(b, int) and b == 0)

        def splits_next(b, kind, s, outs):
            last = kind == "last" and s == 1
            return (outs or last and isinstance(b, int) and b == 1) and not (
                last and isinstance(b, int) and b == B + 1)

        def load_vec(eng, n):
            name, i = ("b", "g", "be", "m", "v")[n // 3], n % 3
            eng.dma_start(vec_rows[n:n + 1, 0:K], layers[i][name].rearrange("(a k) -> a k", a=1)
                          ).then_inc(vecs_loaded, 16)

        @block.sync
        def _(sp):
            def load(g, s):
                wait(sp, x_turned, 4 * (2 * g + s - 1))
                sp.dma_start(xs[:, s].rearrange("p ct h n -> p ct (h n)"),
                             x_view[g // UNITS, :, :, bass.ds((2 * (g % UNITS) + s) * 2 * CH, 2 * CH)]
                             ).then_inc(x_loaded[s], 16)

            def store(g, s):
                for h in range(2):
                    for ct in range(CT):
                        sp.wait_ge(out_evac[ct], 2 * (2 * g + s) + h + 1)
                    sp.dma_start(out_view[g // UNITS, :, :, bass.ds((4 * (g % UNITS) + 2 * s + h) * CH, CH)],
                                 out_s[:, s, h]).then_inc(out_stored[s][h], 16)

            lag = 2 * UNITS + 1
            load(0, 0)
            for n in range(8, 15):
                load_vec(sp, n)
            load(0, 1)
            with sp.Fori(1, lag) as g:
                load(g, 0)
                load(g, 1)
            with sp.Fori(lag, B * UNITS) as g:
                store(g - lag, 0)
                load(g, 0)
                store(g - lag, 1)
                load(g, 1)
            with sp.Fori(B * UNITS - lag, B * UNITS) as g:
                store(g, 0)
                store(g, 1)
            for s in range(2):
                for h in range(2):
                    sp.wait_ge(out_stored[s][h], 16 * B * UNITS)

        @block.gpsimd
        def _(pool):
            nc.gpsimd.memset(ident[:], 0.0).then_inc(ident_zeroed, 1)
            nc.gpsimd.memset(minus_half[:], -0.5).then_inc(ident_zeroed, 1)
            pool.wait_ge(ident_zeroed, 2)
            nc.gpsimd.affine_select(out=ident[:], in_=ident[:], compare_op=ALU.not_equal, fill=1.0,
                                    base=0, pattern=[[-1, P]], channel_multiplier=1
                                    ).then_inc(ident_ready, 1)
            pool.wait_ge(var_ready, 1)
            nc.gpsimd.tensor_tensor(bn_tmp[:, 1], bn_tmp[:, 0], minus_half[:], ALU.pow
                                    ).then_inc(root_ready, 1)

            def unit(b, u, kind, feats, inv, outs):
                for s in range(2):
                    t = 2 * (b * UNITS + u) + s
                    if inv and kind == "first" and s == 1:
                        pool.wait_ge(rows_summed, b)
                        nc.gpsimd.tensor_tensor(e[:], row_sums[:], minus_half[0:K, 0:1], ALU.pow
                                                ).then_inc(rows_rooted, 1)
                    if feats:
                        pool.wait_ge(act_ready[2], t + 1)
                        if outs:
                            pool.wait_ge(split_done, t - 2 * STEPS + 1)
                        nc.gpsimd.tensor_tensor(s_all[:, bass.ds((t % (2 * STEPS)) * CH, CH)], r[:, s],
                                                o2[:, s], ALU.add).then_inc(s_kept, 1)

            run(pool, unit)

        @block.tensor
        def _(pe):
            pe.wait_ge(ident_ready, 1)
            pe.wait_ge(weights_loaded, 16 * 5)
            for ct in range(CT):
                nc.tensor.transpose(conv_ps[:, 0, ct * K:(ct + 1) * K], w0[:, ct * P:(ct + 1) * P],
                                    ident[0:K, 0:K])
            for i in range(2):
                last = nc.tensor.transpose(conv_ps[:, 1, i * P:(i + 1) * P], w12[:, i], ident[:])
            last.then_inc(weights_turned, 1)
            pe.wait_ge(rows_doubled, 1)
            nc.tensor.transpose(out_ps[:, 0, 0:15], vec_rows[:], ident[0:15, 0:15]).then_inc(vecs_turned, 1)
            pe.wait_ge(weights_ready, 1)

            def inverse_slot(b, slot, n):
                pe.wait_ge(inv_operand, (b - 1) * SLOTS + n + 1)
                if slot == "halves":
                    mm = nc.tensor.matmul(inv_ps[0:K, 0:GW + 2], fold[:], gram_s[:], start=True, stop=True)
                elif slot == "turn":
                    mm = nc.tensor.matmul(inv_ps[0:K, 0:K], square[:], ident[:, 0:K], start=True, stop=True)
                elif slot in (0, 1):
                    for half in range(2):
                        mm = nc.tensor.matmul(inv_ps[half * K:(half + 1) * K, 0:K], powers[:, slot, 0:K],
                                              powers[:, slot, half * K:(half + 1) * K],
                                              start=True, stop=True)
                elif slot == "test":
                    mm = nc.tensor.matmul(inv_ps[0:K, 0:K], scaled[:], powers[:, 0, K:2 * K],
                                          start=True, stop=True)
                elif slot == "fix":
                    mm = nc.tensor.matmul(inv_ps[0:K, 0:K], powers[:, 0, K:2 * K], square[:],
                                          start=True, stop=True)
                else:
                    mm = nc.tensor.matmul(inv_ps[0:K, 0:C], powers[:, 0, K:2 * K], target[:],
                                          start=True, stop=True)
                mm.then_inc(inv_product, 1)

            def unit(b, u, kind, feats, inv, outs):
                for s in range(2):
                    t = 2 * (b * UNITS + u) + s
                    tc = t - 2 * STEPS
                    prev = turns_last(b, kind, s, feats)
                    slots = slots_of(kind, u, s) if inv else {}

                    def conv0():
                        pe.wait_ge(x_loaded[s], 16 * (b * UNITS + u + 1))
                        wait(pe, y_ready[1], t)
                        for ct in range(CT):
                            for h in range(2):
                                mm = nc.tensor.matmul(conv_ps[h * K:(h + 1) * K, 0, :], w0T[:, ct],
                                                      xs[:, s, ct, h], start=(ct == 0), stop=(ct == CT - 1))
                        mm.then_inc(conv_ready[0], 1)

                    def conv1():
                        pe.wait_ge(act_ready[0], t + 1)
                        nc.tensor.matmul(conv_ps[:, 0, :], w12T[:, 0], r[:, s], start=True, stop=True
                                         ).then_inc(conv_ready[1], 1)

                    def conv2():
                        pe.wait_ge(act_ready[1], t + 1)
                        wait(pe, s_evac, t)
                        nc.tensor.matmul(conv_ps[:, 1, :], w12T[:, 1], o1[:], start=True, stop=True
                                         ).then_inc(conv_ready[2], 1)

                    def turn_x(q):
                        if q == 0:
                            wait(pe, x_evac_act, t)
                        elif q == 1:
                            wait(pe, x_evac_dve, 3 * t)
                        else:
                            pe.wait_ge(x_evac_dve, 3 * t + q - 1)
                        for h in range(2):
                            for ct in range(CT):
                                mm = nc.tensor.transpose(turn_ps[:, q % 2, (h * CT + ct) * P:(h * CT + ct + 1) * P],
                                                         xs[:, s, ct, h, q * P:(q + 1) * P], ident[:])
                        mm.then_inc(x_turned, 1)

                    def turn_s():
                        pe.wait_ge(s_ready, t)
                        for q in range(Q):
                            mm = nc.tensor.transpose(conv_ps[:, 1, q * P:(q + 1) * P],
                                                     s_now[:, 1 - s, q * P:(q + 1) * P], ident[:])
                        mm.then_inc(s_turned, 1)

                    def gram_of(q):
                        if q == 0:
                            pe.wait_ge(s_evac, t)
                            pe.wait_ge(x_evac_dve, 3 * t)
                            pe.wait_ge(x_evac_act, t)
                        first = kind == "first" and s == 1 and q == 0
                        last = kind == "first" and s == 0 and q == Q - 1
                        if first:
                            wait(pe, gram_saved, b)
                        for h in range(2):
                            mm = nc.tensor.matmul(gram_ps[h * K:(h + 1) * K, 0:GW],
                                                  turned[:, 1 - s, q, h, C:GW], turned[:, 1 - s, q, h, :],
                                                  start=first, stop=last)
                        if q == Q - 1:
                            mm.then_inc(gram_done, 1)

                    def output(k):
                        h, ct = k // CT, k % CT
                        if k == 0:
                            pe.wait_ge(split_done, tc + 1)
                            if kind == "first" and s == 0:
                                pe.wait_ge(proj_split, b - 1)
                        wait(pe, out_evac[k % 2], 2 * tc + k // 2)
                        nc.tensor.matmul(out_ps[:, k % 2, :], proj_hi[:, ct * P:(ct + 1) * P],
                                         s_split[:, s, h], start=True, stop=False)
                        mm = nc.tensor.matmul(out_ps[:, k % 2, :], proj_lo[:, ct * P:(ct + 1) * P],
                                              s_split[:, s, h], start=False, stop=True)
                        mm.then_inc(out_ready[s], 1)

                    def inverse(place):
                        if place in slots:
                            n = slots[place]
                            if kind == "mid":
                                what = 0 if place == 1 else 1
                            elif n == PROJECT:
                                what = "project"
                            elif n >= FIRST_FIX:
                                what = ("test", "fix")[(n - FIRST_FIX) % 2]
                            else:
                                what = "halves" if n == SUM_HALVES else "turn"
                            inverse_slot(b, what, n)

                    if outs and kind == "first" and s == 0:
                        pe.wait_ge(proj_ready, b - 1)
                        nc.tensor.matmul(inv_ps[:, 0:C], spread[:], proj[:], start=True, stop=True
                                         ).then_inc(proj_spread, 1)
                    if feats:
                        conv0()
                        turn_x(0)
                    if outs:
                        output(0)
                    if prev:
                        turn_s()
                    inverse(0)
                    if feats:
                        turn_x(1)
                    if outs:
                        output(1)
                    if feats:
                        conv1()
                    inverse(1)
                    if prev:
                        gram_of(0)
                    if feats:
                        turn_x(2)
                    if prev:
                        gram_of(1)
                    if outs:
                        output(2)
                    if feats:
                        conv2()
                    inverse(2)
                    if prev:
                        gram_of(2)
                    if outs:
                        output(3)
                    if feats:
                        turn_x(3)
                    if prev:
                        gram_of(3)
                    inverse(3)

            run(pe, unit)

        @block.scalar
        def _(act):
            act.wait_ge(w12_zeroed, 1)
            act.dma_start(w0[:], layers[0]["w"]).then_inc(weights_loaded, 16)
            for i in range(2):
                for h in range(2):
                    act.dma_start(w12[h * K:(h + 1) * K, i, h * K:(h + 1) * K],
                                  layers[1 + i]["w"]).then_inc(weights_loaded, 16)
            for n in range(8):
                load_vec(act, n)
            act.wait_ge(const_ready, 1)

            def unit(b, u, kind, feats, inv, outs):
                for s in range(2):
                    g = b * UNITS + u
                    t = 2 * g + s
                    tc = t - 2 * STEPS
                    prev = turns_last(b, kind, s, feats)

                    def normalise(i):
                        act.wait_ge(conv_ready[i], t + 1)
                        wait(act, act_ready[i], t)
                        nc.scalar.activation(y[:, i], conv_ps[:, i // 2, :], ACT.Identity,
                                             bias=bn_bias[:, i:i + 1], scale=bn_scale[:, i:i + 1]
                                             ).then_inc(y_ready[i], 1)

                    def evac_output(k):
                        h, ct = k // CT, k % CT
                        act.wait_ge(out_ready[s], 4 * (g - 2 * UNITS) + k + 1)
                        if ct == 0:
                            wait(act, out_stored[s][h], 16 * (g - 2 * UNITS))
                        nc.scalar.activation(out_s[:, s, h, ct], out_ps[:, k % 2, :], ACT.Copy
                                             ).then_inc(out_evac[k % 2], 1)

                    if feats:
                        normalise(0)
                    if outs:
                        evac_output(0)
                    if prev:
                        act.wait_ge(s_turned, t)
                        nc.scalar.activation(
                            turned[:, 1 - s].rearrange("p q h c -> p (q h) c")[:, :, C:GW],
                            conv_ps[:, 1, :].rearrange("p (a k) -> p a k", k=K), ACT.Copy
                        ).then_inc(s_evac, 1)
                    if outs:
                        evac_output(1)
                    if feats:
                        normalise(1)
                        act.wait_ge(x_turned, 4 * t + 3)
                        wait(act, gram_done, t - 1)
                        nc.scalar.activation(turned[:, s, 2, :, 0:C],
                                             turn_ps[:, 0, :].rearrange("p (h c) -> p h c", h=2), ACT.Copy
                                             ).then_inc(x_evac_act, 1)
                    if outs:
                        evac_output(2)
                    if feats:
                        normalise(2)
                    if outs:
                        evac_output(3)
                    if feats:
                        act.wait_ge(s_ready, t + 1)
                        nc.scalar.activation(abs_out[:], s_now[:, s], ACT.Abs,
                                             accum_out=l1_parts[:, bass.ds(t % (2 * STEPS), 1)]
                                             ).then_inc(abs_done, 1)

            run(act, unit)

        @block.vector
        def _(dve):
            def step(instruction, n):
                instruction.then_inc(const_step, 1)
                dve.wait_ge(const_step, n)

            nc.vector.memset(w12[:], 0.0).then_inc(w12_zeroed, 1)
            for zeroed in (spread, gram_s, square, scaled, powers, target, proj, l1_parts):
                last = nc.vector.memset(zeroed[:], 0.0)
            step(last, 1)
            dve.wait_ge(ident_ready, 1)
            nc.vector.tensor_tensor(fold[:], ident[:, 0:K], ident[:, K:P], ALU.add)
            for half in range(2):
                nc.vector.tensor_copy(spread[0:K, half * K:(half + 1) * K], ident[0:K, 0:K])
            dve.wait_ge(weights_turned, 1)
            nc.vector.tensor_copy(w0T[:], conv_ps[:, 0, 0:CT * K].rearrange("p (c k) -> p c k", c=CT))
            nc.vector.tensor_copy(w12T[:], conv_ps[:, 1, 0:2 * P].rearrange("p (c k) -> p c k", c=2)
                                  ).then_inc(weights_ready, 1)
            dve.wait_ge(vecs_loaded, 16 * 15)
            nc.vector.tensor_copy(vec_rows[:, K:P], vec_rows[:, 0:K]).then_inc(rows_doubled, 1)
            dve.wait_ge(vecs_turned, 1)
            step(nc.vector.tensor_copy(vecs[:], out_ps[:, 0, 0:15].rearrange("p (a i) -> p a i", i=3)), 2)
            nc.vector.tensor_scalar(bn_tmp[:, 0], vecs[:, 4], BN_EPS, None, ALU.add).then_inc(var_ready, 1)
            dve.wait_ge(root_ready, 1)
            nc.vector.tensor_tensor(bn_scale[:], vecs[:, 1], bn_tmp[:, 1], ALU.mult)
            step(nc.vector.tensor_tensor(bn_bias[:], vecs[:, 0], vecs[:, 3], ALU.subtract), 3)
            step(nc.vector.tensor_tensor(bn_bias[:], bn_bias[:], bn_scale[:], ALU.mult), 4)
            nc.vector.tensor_tensor(bn_bias[:], bn_bias[:], vecs[:, 2], ALU.add).then_inc(const_ready, 1)

            def take_in(b, slot, n):
                base = (b - 1) * CHAIN
                dve.wait_ge(inv_product, (b - 1) * SLOTS + n + 1)
                if slot == "halves":
                    nc.vector.tensor_copy(gram[:], inv_ps[0:K, 0:GW + 2]).then_inc(inv_step, 1)
                    dve.wait_ge(inv_step, base + 1)
                    nc.vector.tensor_scalar(l1e[:], gram[:, GW:GW + 1], L1_EPS, None, ALU.add
                                            ).then_inc(inv_step, 1)
                    dve.wait_ge(inv_step, base + 2)
                    nc.vector.reciprocal(d[:], l1e[:]).then_inc(inv_step, 1)
                    dve.wait_ge(inv_step, base + 3)
                    nc.vector.tensor_scalar(square[0:K], gram[:, C:GW], d[:], None, ALU.mult
                                            ).then_inc(inv_operand, 1)
                elif slot == "turn_gram":
                    nc.vector.tensor_scalar(amat[:], inv_ps[0:K, 0:K], d[:], None, ALU.mult
                                            ).then_inc(inv_step, 1)
                    dve.wait_ge(inv_step, base + 4)
                    nc.vector.tensor_reduce(row_sums[:], amat[:], AX.X, ALU.add, apply_absolute_value=True
                                            ).then_inc(rows_summed, 1)
                    dve.wait_ge(rows_rooted, b)
                    nc.vector.tensor_tensor(de[:], d[:], e[:], ALU.mult).then_inc(inv_step, 1)
                    nc.vector.tensor_scalar(square[0:K], amat[:], e[:], None, ALU.mult
                                            ).then_inc(inv_operand, 1)
                elif slot == "turn_scaled":
                    nc.vector.tensor_scalar(scaled[0:K], inv_ps[0:K, 0:K], e[:], None, ALU.mult
                                            ).then_inc(inv_step, 1)
                    nc.vector.tensor_copy(powers[0:K, 0, K:2 * K], ident[0:K, 0:K]).then_inc(inv_step, 1)
                    dve.wait_ge(inv_step, base + 7)
                    nc.vector.tensor_scalar(target[0:K], gram[:, 0:C], de[:], None, ALU.mult
                                            ).then_inc(inv_step, 1)
                    dve.wait_ge(inv_step, base + 8)
                    nc.vector.scalar_tensor_tensor(out=powers[0:K, 0, 0:K], in0=scaled[0:K], scalar=-1.0,
                                                   in1=ident[0:K, 0:K], op0=ALU.mult, op1=ALU.add
                                                   ).then_inc(inv_operand, 1)
                elif slot in (0, 1):
                    nc.vector.tensor_tensor(powers[0:K, 1 - slot, K:2 * K], inv_ps[K:2 * K, 0:K],
                                            powers[0:K, slot, K:2 * K], ALU.add)
                    nc.vector.tensor_copy(powers[0:K, 1 - slot, 0:K], inv_ps[0:K, 0:K]
                                          ).then_inc(inv_operand, 1)
                elif slot == "test":
                    nc.vector.scalar_tensor_tensor(out=square[0:K], in0=inv_ps[0:K, 0:K], scalar=-1.0,
                                                   in1=ident[0:K, 0:K], op0=ALU.mult, op1=ALU.add
                                                   ).then_inc(inv_operand, 1)
                elif slot == "fix":
                    nc.vector.tensor_tensor(powers[0:K, 0, K:2 * K], inv_ps[0:K, 0:K],
                                            powers[0:K, 0, K:2 * K], ALU.add).then_inc(inv_operand, 1)
                else:
                    nc.vector.tensor_scalar(proj[0:K], inv_ps[0:K, 0:C], de[:], None, ALU.mult
                                            ).then_inc(proj_ready, 1)

            def unit(b, u, kind, feats, inv, outs):
                for s in range(2):
                    g = b * UNITS + u
                    t = 2 * g + s
                    tc = t - 2 * STEPS
                    slots = slots_of(kind, u, s) if inv else {}

                    def inverse(place):
                        if place in slots:
                            n = slots[place]
                            if kind == "mid":
                                what = 0 if place == 1 else 1
                            elif n == PROJECT:
                                what = "project"
                            elif n >= FIRST_FIX:
                                what = ("test", "fix")[(n - FIRST_FIX) % 2]
                            else:
                                what = {SUM_HALVES: "halves", TURN_GRAM: "turn_gram",
                                        TURN_SCALED: "turn_scaled"}[n]
                            take_in(b, what, n)

                    def evac_x(q):
                        dve.wait_ge(x_turned, 4 * t + q + 1)
                        if q == 0:
                            wait(dve, gram_done, t - 1)
                        nc.vector.tensor_copy(turned[:, s, q, :, 0:C],
                                              turn_ps[:, q % 2, :].rearrange("p (h c) -> p h c", h=2)
                                              ).then_inc(x_evac_dve, 1)

                    def split_next():
                        o = 1 - s
                        wait(dve, out_ready[o], 4 * (g - 2 * UNITS + s))
                        dve.wait_ge(s_kept, tc + 2)
                        place = bass.ds(((t + 1) % (2 * STEPS)) * CH, CH)
                        for h in range(2):
                            nc.vector.tensor_copy(s_split[h * K:(h + 1) * K, o, h],
                                                  s_all[h * K:(h + 1) * K, place]).then_inc(split_hi, 1)
                        dve.wait_ge(split_hi, 2 * tc + 4)
                        for h in range(2):
                            low = nc.vector.tensor_tensor(
                                s_split[(1 - h) * K:(2 - h) * K, o, h], s_all[h * K:(h + 1) * K, place],
                                s_split[h * K:(h + 1) * K, o, h].bitcast(F32), ALU.subtract)
                        low.then_inc(split_done, 1)

                    def leaky(i, dst):
                        dve.wait_ge(y_ready[i], t + 1)
                        nc.vector.scalar_tensor_tensor(out=dst, in0=y[:, i], scalar=SLOPE, in1=y[:, i],
                                                       op0=ALU.mult, op1=ALU.max).then_inc(act_ready[i], 1)

                    if outs and kind == "first" and s == 0:
                        dve.wait_ge(proj_spread, b - 1)
                        wait(dve, out_ready[1], 4 * UNITS * (b - 2))
                        nc.vector.tensor_copy(proj_hi[:], inv_ps[:, 0:C]).then_inc(proj_hi_ready, 1)
                        dve.wait_ge(proj_hi_ready, b - 1)
                        nc.vector.tensor_tensor(proj_lo[:], inv_ps[:, 0:C], proj_hi[:].bitcast(F32),
                                                ALU.subtract).then_inc(proj_split, 1)
                    if feats:
                        evac_x(0)
                        wait(dve, conv_ready[1], t - 1)
                        wait(dve, s_kept, t - 1)
                        leaky(0, r[:, s])
                    inverse(0)
                    if feats:
                        evac_x(1)
                    inverse(1)
                    if feats:
                        wait(dve, conv_ready[2], t)
                        leaky(1, o1[:])
                    if splits_next(b, kind, s, outs):
                        split_next()
                    inverse(2)
                    if feats:
                        leaky(2, o2[:, s])
                        dve.wait_ge(act_ready[2], t + 1)
                        wait(dve, s_turned, t - 1)
                        wait(dve, abs_done, t - 1)
                        nc.vector.tensor_tensor(s_now[:, s], r[:, s], o2[:, s], ALU.add
                                                ).then_inc(s_ready, 1)
                        evac_x(3)
                    inverse(3)
                    if inv and kind == "first" and s == 0:
                        dve.wait_ge(gram_done, STEPS * b)
                        nc.vector.tensor_copy(gram_s[:, 0:GW], gram_ps[:, 0:GW]).then_inc(gram_saved, 1)
                        dve.wait_ge(abs_done, STEPS * b)
                        nc.vector.tensor_reduce(
                            gram_s[:, GW:GW + 1], l1_parts[:, bass.ds(((b + 1) % 2) * STEPS, STEPS)],
                            AX.X, ALU.add).then_inc(inv_operand, 1)

            run(dve, unit)


_VECS = ("w", "b", "g", "be", "m", "v")


def kernel(**inputs):
    import numpy as _np
    import concourse.bacc as _bacc
    from concourse import mybir as _mybir
    from concourse.bass_utils import run_bass_kernel_spmd as _run

    nc = _bacc.Bacc("TRN2", target_bir_lowering=False, num_devices=1)
    arrays, aps = {}, {}
    for name in ["x"] + [f"L0_conv_{v}{i}" for i in range(3) for v in _VECS]:
        a = _np.ascontiguousarray(inputs[name])
        arrays[f"in_{name}"] = a
        aps[name] = nc.dram_tensor(f"in_{name}", a.shape, _mybir.dt.from_np(a.dtype), kind="ExternalInput").ap()
    out = nc.dram_tensor("out", arrays["in_x"].shape, _mybir.dt.float32, kind="ExternalOutput").ap()
    layers = [{v: aps[f"L0_conv_{v}{i}"] for v in _VECS} for i in range(3)]
    projection_kernel(nc, aps["x"], layers, out)
    r = _run(nc, [arrays], core_ids=[0])
    return r.results[0]["out"]
```

```python
from contextlib import ExitStack

import concourse.bass as bass
from concourse import mybir

F32 = mybir.dt.float32
F32R = mybir.dt.float32r
ACT = mybir.ActivationFunctionType
ALU = mybir.AluOpType
AX = mybir.AxisListType

P = 128
BN_EPS = 1e-5
L1_EPS = 1e-6
SLOPE = 0.1

SUM_HALVES, TURN_GRAM, TURN_SCALED, FIRST_POWER = 0, 1, 2, 3
POWERS = 24
FIRST_FIX = FIRST_POWER + POWERS
FIXES = 3
PROJECT = FIRST_FIX + 2 * FIXES
SLOTS = PROJECT + 1
CHAIN = 8


def projection_kernel(nc, x, layers, out):
    B, C, H, W = x.shape
    K = layers[0]["w"].shape[0]
    N = H * W
    HALF = N // 2
    CH = 512
    STEPS = HALF // CH
    UNITS = STEPS // 2
    CT = C // P
    Q = CH // P
    GW = C + K
    assert K == 64 and CT == 2 and UNITS == 8 and Q == 4

    x_view = x.rearrange("b (ct c) h w -> b c ct (h w)", ct=CT)
    out_view = out.rearrange("b (ct c) h w -> b c ct (h w)", ct=CT)

    with ExitStack() as ctx:
        def sb(name, shape, dt=F32):
            return ctx.enter_context(nc.sbuf_tensor(name, shape, dt))

        def sem(name):
            return ctx.enter_context(nc.semaphore(name))

        ident = sb("ident", [P, P])
        fold = sb("fold", [P, K])
        spread = sb("spread", [P, P])
        minus_half = sb("minus_half", [P, 3])
        vec_rows = sb("vec_rows", [15, P])
        vecs = sb("vecs", [P, 5, 3])
        bn_scale = sb("bn_scale", [P, 3])
        bn_bias = sb("bn_bias", [P, 3])
        bn_tmp = sb("bn_tmp", [P, 2, 3])
        w0 = sb("w0", [K, C])
        w12 = sb("w12", [P, 2, P])
        w0T = sb("w0T", [P, CT, K])
        w12_hi = sb("w12_hi", [P, 2, P], F32R)
        w12_lo = sb("w12_lo", [P, 2, P], F32R)

        xs = sb("xs", [P, 2, CT, 2, CH])
        y = sb("y", [P, 3, CH])
        r = sb("r", [P, 2, CH])
        o1 = sb("o1", [P, CH])
        act_hi = sb("act_hi", [P, 2, CH], F32R)
        act_lo = sb("act_lo", [P, 2, CH], F32R)
        o2 = sb("o2", [P, 2, CH])
        s_now = sb("s_now", [P, 2, CH])
        s_all = sb("s_all", [P, 2 * STEPS * CH])
        abs_out = sb("abs_out", [P, CH])
        l1_parts = sb("l1_parts", [P, 2 * STEPS])
        turned = sb("turned", [P, 2, Q, 2, GW])
        gram_s = sb("gram_s", [P, GW + 2])
        gram = sb("gram", [K, GW + 2])
        l1e = sb("l1e", [K, 1])
        d = sb("d", [K, 1])
        row_sums = sb("row_sums", [K, 1])
        e = sb("e", [K, 1])
        de = sb("de", [K, 1])
        amat = sb("amat", [K, K])
        square = sb("square", [P, K])
        scaled = sb("scaled", [P, K])
        powers = sb("powers", [P, 2, 2 * K])
        target = sb("target", [P, C])
        proj = sb("proj", [P, C])
        proj_hi = sb("proj_hi", [P, C], F32R)
        proj_lo = sb("proj_lo", [P, C], F32R)
        s_split = sb("s_split", [P, 2, 2, CH], F32R)
        out_s = sb("out_s", [P, 2, 2, CT, CH])

        gram_ps = ctx.enter_context(nc.psum_tensor("gram_ps", [P, CH], F32))
        conv_ps = ctx.enter_context(nc.psum_tensor("conv_ps", [P, 2, CH], F32))
        turn_ps = ctx.enter_context(nc.psum_tensor("turn_ps", [P, 2, CH], F32))
        out_ps = ctx.enter_context(nc.psum_tensor("out_ps", [P, 2, CH], F32))
        inv_ps = ctx.enter_context(nc.psum_tensor("inv_ps", [P, CH], F32))

        weights_loaded = sem("weights_loaded")
        vecs_loaded = sem("vecs_loaded")
        rows_doubled = sem("rows_doubled")
        vecs_turned = sem("vecs_turned")
        w12_zeroed = sem("w12_zeroed")
        ident_zeroed = sem("ident_zeroed")
        ident_ready = sem("ident_ready")
        var_ready = sem("var_ready")
        root_ready = sem("root_ready")
        const_step = sem("const_step")
        const_ready = sem("const_ready")
        weights_turned = sem("weights_turned")
        weights_ready = sem("weights_ready")
        x_loaded = [sem("x_loaded0"), sem("x_loaded1")]
        conv_ready = [sem(f"conv{i}_ready") for i in range(3)]
        y_ready = [sem(f"y{i}_ready") for i in range(3)]
        act_ready = [sem(f"act{i}_ready") for i in range(3)]
        act_hi_ready = [sem(f"act{i}_hi_ready") for i in range(2)]
        act_lo_ready = [sem(f"act{i}_lo_ready") for i in range(2)]
        s_ready = sem("s_ready")
        s_kept = sem("s_kept")
        abs_done = sem("abs_done")
        x_turned = sem("x_turned")
        x1_evac = sem("x1_evac")
        x_evac = sem("x_evac")
        s_turned = sem("s_turned")
        s_evac = sem("s_evac")
        gram_done = sem("gram_done")
        gram_saved = sem("gram_saved")
        inv_operand = sem("inv_operand")
        inv_product = sem("inv_product")
        inv_step = sem("inv_step")
        rows_summed = sem("rows_summed")
        rows_rooted = sem("rows_rooted")
        proj_ready = sem("proj_ready")
        proj_spread = sem("proj_spread")
        proj_hi_ready = sem("proj_hi_ready")
        proj_split = sem("proj_split")
        split_hi = sem("split_hi")
        split_done = [sem("split_done0"), sem("split_done1")]
        out_ready = [sem("out_ready0"), sem("out_ready1")]
        out_evac = [sem("out_evac0"), sem("out_evac1")]
        out_stored = [[sem(f"out_stored{s}{h}") for h in range(2)] for s in range(2)]

        block = ctx.enter_context(nc.Block())

        def wait(eng, s, value):
            if not isinstance(value, int) or value > 0:
                eng.wait_ge(s, value)

        def run(eng, unit):
            unit(0, 0, "first", True, False, False)
            with eng.Fori(1, UNITS) as u:
                unit(0, u, "mid", True, False, False)
            image(eng, unit, 1, True, True, False)
            image(eng, unit, 2, True, True, True)
            with eng.Fori(3, B) as b:
                image(eng, unit, b, True, True, True)
            image(eng, unit, B, False, True, True)
            image(eng, unit, B + 1, False, False, True)

        def image(eng, unit, b, feats, inv, outs):
            unit(b, 0, "first", feats, inv, outs)
            with eng.Fori(1, UNITS - 1) as u:
                unit(b, u, "mid", feats, inv, outs)
            unit(b, UNITS - 1, "last", feats, inv, outs)

        def slots_of(kind, u, s):
            if kind == "first":
                return {1: SUM_HALVES, 2: TURN_GRAM, 3: TURN_SCALED} if s else {}
            if kind == "mid":
                at = FIRST_POWER + 4 * (u - 1) + 2 * s
                return {1: at, 3: at + 1}
            at = FIRST_FIX + 4 * s
            return {place: at + place for place in range(4) if at + place < SLOTS}

        def turns_last(b, kind, s, feats):
            first = kind == "first" and s == 0
            return (feats or first and isinstance(b, int) and b == B) and not (
                first and isinstance(b, int) and b == 0)

        def takes_rows(kind, s, inv):
            return inv and kind == "first" and s == 1

        def splits_next(b, kind, s, outs):
            last = kind == "last" and s == 1
            return (outs or last and isinstance(b, int) and b == 1) and not (
                last and isinstance(b, int) and b == B + 1)

        def load_vec(eng, n):
            name, i = ("b", "g", "be", "m", "v")[n // 3], n % 3
            eng.dma_start(vec_rows[n:n + 1, 0:K], layers[i][name].rearrange("(a k) -> a k", a=1)
                          ).then_inc(vecs_loaded, 16)

        @block.sync
        def _(sp):
            def load(g, s):
                wait(sp, x_turned, 4 * (2 * g + s - 1))
                sp.dma_start(xs[:, s].rearrange("p ct h n -> p ct (h n)"),
                             x_view[g // UNITS, :, :, bass.ds((2 * (g % UNITS) + s) * 2 * CH, 2 * CH)]
                             ).then_inc(x_loaded[s], 16)

            def store(g, s):
                for h in range(2):
                    for ct in range(CT):
                        sp.wait_ge(out_evac[ct], 2 * (2 * g + s) + h + 1)
                    sp.dma_start(out_view[g // UNITS, :, :, bass.ds((4 * (g % UNITS) + 2 * s + h) * CH, CH)],
                                 out_s[:, s, h]).then_inc(out_stored[s][h], 16)

            lag = 2 * UNITS + 1
            load(0, 0)
            for n in range(8, 15):
                load_vec(sp, n)
            load(0, 1)
            with sp.Fori(1, lag) as g:
                load(g, 0)
                load(g, 1)
            with sp.Fori(lag, B * UNITS) as g:
                store(g - lag, 0)
                load(g, 0)
                store(g - lag, 1)
                load(g, 1)
            with sp.Fori(B * UNITS - lag, B * UNITS) as g:
                store(g, 0)
                store(g, 1)
            for s in range(2):
                for h in range(2):
                    sp.wait_ge(out_stored[s][h], 16 * B * UNITS)

        @block.gpsimd
        def _(pool):
            nc.gpsimd.memset(ident[:], 0.0).then_inc(ident_zeroed, 1)
            nc.gpsimd.memset(minus_half[:], -0.5).then_inc(ident_zeroed, 1)
            pool.wait_ge(ident_zeroed, 2)
            nc.gpsimd.affine_select(out=ident[:], in_=ident[:], compare_op=ALU.not_equal, fill=1.0,
                                    base=0, pattern=[[-1, P]], channel_multiplier=1
                                    ).then_inc(ident_ready, 1)
            pool.wait_ge(var_ready, 1)
            nc.gpsimd.tensor_tensor(bn_tmp[:, 1], bn_tmp[:, 0], minus_half[:], ALU.pow
                                    ).then_inc(root_ready, 1)

            def unit(b, u, kind, feats, inv, outs):
                for s in range(2):
                    t = 2 * (b * UNITS + u) + s
                    if inv and kind == "first" and s == 1:
                        pool.wait_ge(rows_summed, b)
                        nc.gpsimd.tensor_tensor(e[:], row_sums[:], minus_half[0:K, 0:1], ALU.pow
                                                ).then_inc(rows_rooted, 1)
                    if feats:
                        pool.wait_ge(act_ready[2], t + 1)
                        if outs:
                            pool.wait_ge(split_done[1], t - 2 * STEPS + 1)
                        nc.gpsimd.tensor_tensor(s_all[:, bass.ds((t % (2 * STEPS)) * CH, CH)], r[:, s],
                                                o2[:, s], ALU.add).then_inc(s_kept, 1)

            run(pool, unit)

        @block.tensor
        def _(pe):
            pe.wait_ge(ident_ready, 1)
            pe.wait_ge(weights_loaded, 16 * 5)
            for ct in range(CT):
                nc.tensor.transpose(conv_ps[:, 0, ct * K:(ct + 1) * K], w0[:, ct * P:(ct + 1) * P],
                                    ident[0:K, 0:K])
            for i in range(2):
                last = nc.tensor.transpose(conv_ps[:, 1, i * P:(i + 1) * P], w12[:, i], ident[:])
            last.then_inc(weights_turned, 1)
            pe.wait_ge(weights_ready, 1)

            def turn_vecs():
                pe.wait_ge(rows_doubled, 1)
                nc.tensor.transpose(out_ps[:, 0, 0:15], vec_rows[:], ident[0:15, 0:15]).then_inc(vecs_turned, 1)

            def inverse_slot(b, slot, n):
                pe.wait_ge(inv_operand, (b - 1) * SLOTS + n + 1)
                if slot == "halves":
                    mm = nc.tensor.matmul(inv_ps[0:K, 0:GW + 2], fold[:], gram_s[:], start=True, stop=True)
                elif slot == "turn":
                    mm = nc.tensor.matmul(inv_ps[0:K, 0:K], square[:], ident[:, 0:K], start=True, stop=True)
                elif slot in (0, 1):
                    for half in range(2):
                        mm = nc.tensor.matmul(inv_ps[half * K:(half + 1) * K, 0:K], powers[:, slot, 0:K],
                                              powers[:, slot, half * K:(half + 1) * K],
                                              start=True, stop=True)
                elif slot == "test":
                    mm = nc.tensor.matmul(inv_ps[0:K, 0:K], scaled[:], powers[:, 0, K:2 * K],
                                          start=True, stop=True)
                elif slot == "fix":
                    mm = nc.tensor.matmul(inv_ps[0:K, 0:K], powers[:, 0, K:2 * K], square[:],
                                          start=True, stop=True)
                else:
                    mm = nc.tensor.matmul(inv_ps[0:K, 0:C], powers[:, 0, K:2 * K], target[:],
                                          start=True, stop=True)
                mm.then_inc(inv_product, 1)

            def unit(b, u, kind, feats, inv, outs):
                for s in range(2):
                    t = 2 * (b * UNITS + u) + s
                    tc = t - 2 * STEPS
                    prev = turns_last(b, kind, s, feats)
                    slots = slots_of(kind, u, s) if inv else {}

                    def conv0():
                        pe.wait_ge(x_loaded[s], 16 * (b * UNITS + u + 1))
                        wait(pe, y_ready[1], t)
                        for ct in range(CT):
                            for h in range(2):
                                mm = nc.tensor.matmul(conv_ps[h * K:(h + 1) * K, 0, :], w0T[:, ct],
                                                      xs[:, s, ct, h], start=(ct == 0), stop=(ct == CT - 1))
                        mm.then_inc(conv_ready[0], 1)

                    def conv_hi(i):
                        pe.wait_ge(act_hi_ready[i - 1], t + 1)
                        if i == 2:
                            wait(pe, s_evac, t)
                        bank = conv_ps[:, i - 1, :]
                        nc.tensor.matmul(bank, w12_lo[:, i - 1], act_hi[:, i - 1], start=True, stop=False)
                        nc.tensor.matmul(bank, w12_hi[:, i - 1], act_hi[:, i - 1], start=False, stop=False)

                    def conv_lo(i):
                        pe.wait_ge(act_lo_ready[i - 1], t + 1)
                        nc.tensor.matmul(conv_ps[:, i - 1, :], w12_hi[:, i - 1], act_lo[:, i - 1],
                                         start=False, stop=True).then_inc(conv_ready[i], 1)

                    def turn_x(q):
                        if q == 3:
                            pe.wait_ge(x1_evac, t + 1)
                        else:
                            wait(pe, x_evac, 3 * t + q - 1)
                        for h in range(2):
                            for ct in range(CT):
                                mm = nc.tensor.transpose(turn_ps[:, q % 2, (h * CT + ct) * P:(h * CT + ct + 1) * P],
                                                         xs[:, s, ct, h, q * P:(q + 1) * P], ident[:])
                        mm.then_inc(x_turned, 1)

                    def turn_s():
                        pe.wait_ge(s_ready, t)
                        for q in range(Q):
                            mm = nc.tensor.transpose(conv_ps[:, 1, q * P:(q + 1) * P],
                                                     s_now[:, 1 - s, q * P:(q + 1) * P], ident[:])
                        mm.then_inc(s_turned, 1)

                    def gram_of(q):
                        if q == 0:
                            pe.wait_ge(s_evac, t)
                            pe.wait_ge(x1_evac, t)
                            pe.wait_ge(x_evac, 3 * t)
                        first = kind == "first" and s == 1 and q == 0
                        last = kind == "first" and s == 0 and q == Q - 1
                        if first:
                            wait(pe, gram_saved, b)
                        for h in range(2):
                            mm = nc.tensor.matmul(gram_ps[h * K:(h + 1) * K, 0:GW],
                                                  turned[:, 1 - s, q, h, C:GW], turned[:, 1 - s, q, h, :],
                                                  start=first, stop=last)
                        if q == Q - 1:
                            mm.then_inc(gram_done, 1)

                    def output(k):
                        h, ct = k // CT, k % CT
                        if ct == 0:
                            pe.wait_ge(split_done[h], tc + 1)
                        if k == 0:
                            if kind == "first" and s == 0:
                                pe.wait_ge(proj_split, b - 1)
                        wait(pe, out_evac[k % 2], 2 * tc + k // 2)
                        nc.tensor.matmul(out_ps[:, k % 2, :], proj_hi[:, ct * P:(ct + 1) * P],
                                         s_split[:, s, h], start=True, stop=False)
                        mm = nc.tensor.matmul(out_ps[:, k % 2, :], proj_lo[:, ct * P:(ct + 1) * P],
                                              s_split[:, s, h], start=False, stop=True)
                        mm.then_inc(out_ready[s], 1)

                    tail = kind == "mid" and not feats

                    def spread_proj():
                        pe.wait_ge(proj_ready, b)
                        nc.tensor.matmul(inv_ps[:, 0:C], spread[:], proj[:], start=True, stop=True
                                         ).then_inc(proj_spread, 1)

                    def inverse(place):
                        if place in slots:
                            n = slots[place]
                            if kind == "mid":
                                what = 0 if place == 1 else 1
                            elif n == PROJECT:
                                what = "project"
                            elif n >= FIRST_FIX:
                                what = ("test", "fix")[(n - FIRST_FIX) % 2]
                            else:
                                what = "halves" if n == SUM_HALVES else "turn"
                            inverse_slot(b, what, n)

                    if feats and not outs:
                        conv0()
                        turn_x(0)
                        if isinstance(t, int) and t == 0:
                            turn_vecs()
                        inverse(0)
                        turn_x(1)
                        if prev:
                            turn_s()
                        inverse(1)
                        turn_x(2)
                        conv_hi(1)
                        if prev:
                            gram_of(0)
                        conv_lo(1)
                        if prev:
                            gram_of(1)
                            gram_of(2)
                        inverse(2)
                        if prev:
                            gram_of(3)
                        turn_x(3)
                        conv_hi(2)
                        inverse(3)
                        conv_lo(2)
                        if inv and kind == "last" and s == 1:
                            spread_proj()
                        continue
                    if feats:
                        conv0()
                        turn_x(0)
                    inverse(0)
                    output(0)
                    if prev:
                        turn_s()
                    inverse(1)
                    if feats:
                        turn_x(1)
                    output(1)
                    if tail:
                        inverse(3)
                    if feats:
                        conv_hi(1)
                        turn_x(2)
                        conv_lo(1)
                    output(2)
                    if prev:
                        gram_of(0)
                        gram_of(1)
                        gram_of(2)
                    if kind == "first":
                        inverse(2)
                    if feats:
                        turn_x(3)
                        conv_hi(2)
                    if kind == "last":
                        inverse(2)
                    output(3)
                    if feats:
                        conv_lo(2)
                    if inv and kind == "last" and s == 1:
                        spread_proj()
                    if prev:
                        gram_of(3)
                    if not tail:
                        inverse(3)

            run(pe, unit)

        @block.scalar
        def _(act):
            act.dma_start(w0[:], layers[0]["w"]).then_inc(weights_loaded, 16)
            act.wait_ge(w12_zeroed, 1)
            for i in range(2):
                for h in range(2):
                    act.dma_start(w12[h * K:(h + 1) * K, i, h * K:(h + 1) * K],
                                  layers[1 + i]["w"]).then_inc(weights_loaded, 16)
            for n in range(8):
                load_vec(act, n)
            act.wait_ge(const_ready, 1)

            def unit(b, u, kind, feats, inv, outs):
                for s in range(2):
                    g = b * UNITS + u
                    t = 2 * g + s
                    tc = t - 2 * STEPS
                    prev = turns_last(b, kind, s, feats)

                    def normalise(i):
                        act.wait_ge(conv_ready[i], t + 1)
                        wait(act, act_ready[i], t)
                        nc.scalar.activation(y[:, i], conv_ps[:, i // 2, :], ACT.Identity,
                                             bias=bn_bias[:, i:i + 1], scale=bn_scale[:, i:i + 1]
                                             ).then_inc(y_ready[i], 1)

                    def evac_output(k):
                        h, ct = k // CT, k % CT
                        act.wait_ge(out_ready[s], 4 * (g - 2 * UNITS) + k + 1)
                        if ct == 0:
                            wait(act, out_stored[s][h], 16 * (g - 2 * UNITS))
                        nc.scalar.activation(out_s[:, s, h, ct], out_ps[:, k % 2, :], ACT.Copy
                                             ).then_inc(out_evac[k % 2], 1)

                    def evac_x(q):
                        act.wait_ge(x_turned, 4 * t + q + 1)
                        if q == 0:
                            wait(act, gram_done, t - 1)
                        nc.scalar.activation(turned[:, s, q, :, 0:C],
                                             turn_ps[:, q % 2, :].rearrange("p (h c) -> p h c", h=2), ACT.Copy
                                             ).then_inc(x1_evac if q == 1 else x_evac, 1)

                    if feats:
                        normalise(0)
                        evac_x(0)
                    if outs:
                        evac_output(0)
                    if prev:
                        act.wait_ge(s_turned, t)
                        nc.scalar.activation(
                            turned[:, 1 - s].rearrange("p q h c -> p (q h) c")[:, :, C:GW],
                            conv_ps[:, 1, :].rearrange("p (a k) -> p a k", k=K), ACT.Copy
                        ).then_inc(s_evac, 1)
                    if feats and takes_rows(kind, s, inv):
                        evac_x(1)
                    if outs:
                        evac_output(1)
                    if prev:
                        act.wait_ge(s_ready, t)
                        nc.scalar.activation(abs_out[:], s_now[:, 1 - s], ACT.Abs,
                                             accum_out=l1_parts[:, bass.ds((t + 2 * STEPS - 1) % (2 * STEPS), 1)]
                                             ).then_inc(abs_done, 1)
                    if feats:
                        normalise(1)
                        evac_x(2)
                    if outs:
                        evac_output(2)
                    if feats:
                        evac_x(3)
                    if feats:
                        normalise(2)
                    if outs:
                        evac_output(3)

            run(act, unit)

        @block.vector
        def _(dve):
            def step(instruction, n):
                instruction.then_inc(const_step, 1)
                dve.wait_ge(const_step, n)

            nc.vector.memset(w12[:], 0.0).then_inc(w12_zeroed, 1)
            for zeroed in (spread, gram_s, square, scaled, powers, target, proj, l1_parts):
                last = nc.vector.memset(zeroed[:], 0.0)
            step(last, 1)
            dve.wait_ge(ident_ready, 1)
            nc.vector.tensor_tensor(fold[:], ident[:, 0:K], ident[:, K:P], ALU.add)
            for half in range(2):
                nc.vector.tensor_copy(spread[0:K, half * K:(half + 1) * K], ident[0:K, 0:K])
            dve.wait_ge(weights_turned, 1)
            nc.vector.tensor_copy(w0T[:], conv_ps[:, 0, 0:CT * K].rearrange("p (c k) -> p c k", c=CT))
            turned_weights = conv_ps[:, 1, 0:2 * P].rearrange("p (c k) -> p c k", c=2)
            step(nc.vector.tensor_copy(w12_hi[:], turned_weights), 2)
            nc.vector.tensor_tensor(w12_lo[:], turned_weights, w12_hi[:].bitcast(F32), ALU.subtract
                                    ).then_inc(weights_ready, 1)
            dve.wait_ge(vecs_loaded, 16 * 15)
            nc.vector.tensor_copy(vec_rows[:, K:P], vec_rows[:, 0:K]).then_inc(rows_doubled, 1)
            dve.wait_ge(vecs_turned, 1)
            step(nc.vector.tensor_copy(vecs[:], out_ps[:, 0, 0:15].rearrange("p (a i) -> p a i", i=3)), 3)
            nc.vector.tensor_scalar(bn_tmp[:, 0], vecs[:, 4], BN_EPS, None, ALU.add).then_inc(var_ready, 1)
            dve.wait_ge(root_ready, 1)
            nc.vector.tensor_tensor(bn_scale[:], vecs[:, 1], bn_tmp[:, 1], ALU.mult)
            step(nc.vector.tensor_tensor(bn_bias[:], vecs[:, 0], vecs[:, 3], ALU.subtract), 4)
            step(nc.vector.tensor_tensor(bn_bias[:], bn_bias[:], bn_scale[:], ALU.mult), 5)
            nc.vector.tensor_tensor(bn_bias[:], bn_bias[:], vecs[:, 2], ALU.add).then_inc(const_ready, 1)

            def take_in(b, slot, n):
                base = (b - 1) * CHAIN
                if slot != "rows_rooted":
                    dve.wait_ge(inv_product, (b - 1) * SLOTS + n + 1)
                if slot == "halves":
                    nc.vector.tensor_copy(gram[:], inv_ps[0:K, 0:GW + 2]).then_inc(inv_step, 1)
                    dve.wait_ge(inv_step, base + 1)
                    nc.vector.tensor_scalar(l1e[:], gram[:, GW:GW + 1], L1_EPS, None, ALU.add
                                            ).then_inc(inv_step, 1)
                    dve.wait_ge(inv_step, base + 2)
                    nc.vector.reciprocal(d[:], l1e[:]).then_inc(inv_step, 1)
                    dve.wait_ge(inv_step, base + 3)
                    nc.vector.tensor_scalar(square[0:K], gram[:, C:GW], d[:], None, ALU.mult
                                            ).then_inc(inv_operand, 1)
                elif slot == "turn_gram":
                    nc.vector.tensor_scalar(amat[:], inv_ps[0:K, 0:K], d[:], None, ALU.mult
                                            ).then_inc(inv_step, 1)
                    dve.wait_ge(inv_step, base + 4)
                    nc.vector.tensor_reduce(row_sums[:], amat[:], AX.X, ALU.add, apply_absolute_value=True
                                            ).then_inc(rows_summed, 1)
                elif slot == "rows_rooted":
                    dve.wait_ge(rows_rooted, b)
                    nc.vector.tensor_tensor(de[:], d[:], e[:], ALU.mult).then_inc(inv_step, 1)
                    nc.vector.tensor_scalar(square[0:K], amat[:], e[:], None, ALU.mult
                                            ).then_inc(inv_operand, 1)
                    nc.vector.tensor_copy(powers[0:K, 0, K:2 * K], ident[0:K, 0:K]).then_inc(inv_step, 1)
                elif slot == "turn_scaled":
                    nc.vector.tensor_scalar(scaled[0:K], inv_ps[0:K, 0:K], e[:], None, ALU.mult
                                            ).then_inc(inv_step, 1)
                    dve.wait_ge(inv_step, base + 7)
                    nc.vector.scalar_tensor_tensor(out=powers[0:K, 0, 0:K], in0=scaled[0:K], scalar=-1.0,
                                                   in1=ident[0:K, 0:K], op0=ALU.mult, op1=ALU.add
                                                   ).then_inc(inv_operand, 1)
                    nc.vector.tensor_scalar(target[0:K], gram[:, 0:C], de[:], None, ALU.mult
                                            ).then_inc(inv_step, 1)
                elif slot in (0, 1):
                    nc.vector.tensor_tensor(powers[0:K, 1 - slot, K:2 * K], inv_ps[K:2 * K, 0:K],
                                            powers[0:K, slot, K:2 * K], ALU.add)
                    nc.vector.tensor_copy(powers[0:K, 1 - slot, 0:K], inv_ps[0:K, 0:K]
                                          ).then_inc(inv_operand, 1)
                elif slot == "test":
                    nc.vector.scalar_tensor_tensor(out=square[0:K], in0=inv_ps[0:K, 0:K], scalar=-1.0,
                                                   in1=ident[0:K, 0:K], op0=ALU.mult, op1=ALU.add
                                                   ).then_inc(inv_operand, 1)
                elif slot == "fix":
                    nc.vector.tensor_tensor(powers[0:K, 0, K:2 * K], inv_ps[0:K, 0:K],
                                            powers[0:K, 0, K:2 * K], ALU.add).then_inc(inv_operand, 1)
                else:
                    nc.vector.tensor_scalar(proj[0:K], inv_ps[0:K, 0:C], de[:], None, ALU.mult
                                            ).then_inc(proj_ready, 1)

            def unit(b, u, kind, feats, inv, outs):
                for s in range(2):
                    g = b * UNITS + u
                    t = 2 * g + s
                    tc = t - 2 * STEPS
                    slots = slots_of(kind, u, s) if inv else {}

                    def inverse(place):
                        if place in slots:
                            n = slots[place]
                            if kind == "mid":
                                what = 0 if place == 1 else 1
                            elif n == PROJECT:
                                what = "project"
                            elif n >= FIRST_FIX:
                                what = ("test", "fix")[(n - FIRST_FIX) % 2]
                            else:
                                what = {SUM_HALVES: "halves", TURN_GRAM: "turn_gram",
                                        TURN_SCALED: "turn_scaled"}[n]
                            take_in(b, what, n)

                    def evac_x1():
                        dve.wait_ge(x_turned, 4 * t + 2)
                        wait(dve, gram_done, t - 1)
                        nc.vector.tensor_copy(turned[:, s, 1, :, 0:C],
                                              turn_ps[:, 1, :].rearrange("p (h c) -> p h c", h=2)
                                              ).then_inc(x1_evac, 1)

                    def split_next(half):
                        o = 1 - s
                        place = bass.ds(((t + 1) % (2 * STEPS)) * CH, CH)
                        if half == 0:
                            wait(dve, out_ready[o], 4 * (g - 2 * UNITS + s))
                            dve.wait_ge(s_kept, tc + 2)
                        nc.vector.tensor_copy(s_split[half * K:(half + 1) * K, o, half],
                                              s_all[half * K:(half + 1) * K, place]).then_inc(split_hi, 1)
                        dve.wait_ge(split_hi, 2 * tc + half + 3)
                        nc.vector.tensor_tensor(
                            s_split[(1 - half) * K:(2 - half) * K, o, half],
                            s_all[half * K:(half + 1) * K, place],
                            s_split[half * K:(half + 1) * K, o, half].bitcast(F32), ALU.subtract
                        ).then_inc(split_done[half], 1)

                    def parts(i, src):
                        dve.wait_ge(act_ready[i], t + 1)
                        wait(dve, conv_ready[i + 1], t)
                        nc.vector.tensor_copy(act_hi[:, i], src).then_inc(act_hi_ready[i], 1)
                        dve.wait_ge(act_hi_ready[i], t + 1)
                        nc.vector.tensor_tensor(act_lo[:, i], src, act_hi[:, i].bitcast(F32), ALU.subtract
                                                ).then_inc(act_lo_ready[i], 1)

                    def leaky(i, dst):
                        dve.wait_ge(y_ready[i], t + 1)
                        nc.vector.scalar_tensor_tensor(out=dst, in0=y[:, i], scalar=SLOPE, in1=y[:, i],
                                                       op0=ALU.mult, op1=ALU.max).then_inc(act_ready[i], 1)

                    inverse(0)
                    if feats:
                        wait(dve, s_kept, t - 1)
                        leaky(0, r[:, s])
                        parts(0, r[:, s])
                    rows = takes_rows(kind, s, inv)
                    if feats and not rows:
                        evac_x1()
                    inverse(1)
                    splits = splits_next(b, kind, s, outs)
                    if splits:
                        split_next(0)
                    tail = kind == "mid" and not feats
                    if tail:
                        inverse(3)
                    if feats:
                        leaky(1, o1[:])
                        parts(1, o1[:])
                    inverse(2)
                    if rows:
                        take_in(b, "rows_rooted", TURN_GRAM)
                    if splits:
                        split_next(1)
                    if inv and kind == "last" and s == 1:
                        dve.wait_ge(proj_spread, b)
                        wait(dve, out_ready[1], 4 * UNITS * (b - 1))
                        nc.vector.tensor_copy(proj_hi[:], inv_ps[:, 0:C]).then_inc(proj_hi_ready, 1)
                        dve.wait_ge(proj_hi_ready, b)
                        nc.vector.tensor_tensor(proj_lo[:], inv_ps[:, 0:C], proj_hi[:].bitcast(F32),
                                                ALU.subtract).then_inc(proj_split, 1)
                    if inv and kind == "first" and s == 0:
                        dve.wait_ge(gram_done, STEPS * b)
                        nc.vector.tensor_copy(gram_s[:, 0:GW], gram_ps[:, 0:GW]).then_inc(gram_saved, 1)
                        dve.wait_ge(abs_done, STEPS * b)
                        nc.vector.tensor_reduce(
                            gram_s[:, GW:GW + 1], l1_parts[:, bass.ds(((b + 1) % 2) * STEPS, STEPS)],
                            AX.X, ALU.add).then_inc(inv_operand, 1)
                    if feats:
                        leaky(2, o2[:, s])
                        dve.wait_ge(act_ready[2], t + 1)
                        wait(dve, s_turned, t - 1)
                        wait(dve, abs_done, t - 1)
                        nc.vector.tensor_tensor(s_now[:, s], r[:, s], o2[:, s], ALU.add
                                                ).then_inc(s_ready, 1)
                    if not tail:
                        inverse(3)

            run(dve, unit)


_VECS = ("w", "b", "g", "be", "m", "v")


def kernel(**inputs):
    import numpy as _np
    import concourse.bacc as _bacc
    from concourse import mybir as _mybir
    from concourse.bass_utils import run_bass_kernel_spmd as _run

    nc = _bacc.Bacc("TRN2", target_bir_lowering=False, num_devices=1)
    arrays, aps = {}, {}
    for name in ["x"] + [f"L0_conv_{v}{i}" for i in range(3) for v in _VECS]:
        a = _np.ascontiguousarray(inputs[name])
        arrays[f"in_{name}"] = a
        aps[name] = nc.dram_tensor(f"in_{name}", a.shape, _mybir.dt.from_np(a.dtype), kind="ExternalInput").ap()
    out = nc.dram_tensor("out", arrays["in_x"].shape, _mybir.dt.float32, kind="ExternalOutput").ap()
    layers = [{v: aps[f"L0_conv_{v}{i}"] for v in _VECS} for i in range(3)]
    projection_kernel(nc, aps["x"], layers, out)
    r = _run(nc, [arrays], core_ids=[0])
    return r.results[0]["out"]
```
